# Optimizing a Trainium2 kernel written in Bass

```python
import numpy as np
import jax
import jax.numpy as jnp

def _softmax(x, axis=-1):
    return jax.nn.softmax(x, axis=axis)

def _gelu(x):
    return jax.nn.gelu(x, approximate=True)

def _silu(x):
    return jax.nn.silu(x)

def _sigmoid(x):
    return jax.nn.sigmoid(x)

def _layernorm(x, axis=-1, eps=1e-05):
    m = jnp.mean(x, axis=axis, keepdims=True)
    v = jnp.var(x, axis=axis, keepdims=True)
    return (x - m) / jnp.sqrt(v + eps)

def _scatter_add(tgt, idx, src, axis=0):
    return tgt.at[idx].add(src)

def _segment_sum(src, seg, n):
    return jax.ops.segment_sum(src, seg, n)
kernel_name = 'mk_prb_d1_jaxref_r8_7e50cd'

def setup_inputs(seed: int=0):
    np.random.seed(seed)
    _w = jnp.asarray

    def _L0_attn_setup():
        import jax, jax.numpy as jnp
        import numpy as np
        import math
        B, S, H = (1, 256, 512)
        NH, NKV, HD = (32, 8, 128)
        GS = 128
        WBITS = 4
        ZERO = float(2 ** (WBITS - 1))
        THETA = 10000.0

        def _dequant_matmul(x, qw, scales):
            w = (qw.astype(jnp.float32) - ZERO) * jnp.repeat(scales, GS, axis=0)
            return x @ w

        def _rope_tables(seq_len, dtype):
            inv_freq = 1.0 / THETA ** (jnp.arange(0, HD, 2, dtype=jnp.float32) / HD)
            freqs = jnp.arange(seq_len, dtype=jnp.float32)[:, None] * inv_freq
            emb = jnp.concatenate([freqs, freqs], axis=-1)
            return (jnp.cos(emb).astype(dtype), jnp.sin(emb).astype(dtype))

        def _rotate_half(x):
            x1, x2 = jnp.split(x, 2, axis=-1)
            return jnp.concatenate([-x2, x1], axis=-1)

        def _apply_rope(x, cos, sin):
            return x * cos[None, None] + _rotate_half(x) * sin[None, None]
        key = jax.random.key(seed)
        ks = jax.random.split(key, 9)
        small = lambda k, shp: jax.random.uniform(k, shp, jnp.float32) * 0.01 + 0.001
        return {'hidden_states': jax.random.normal(ks[0], (B, S, H), jnp.float32), 'scales_q': small(ks[1], (H // GS, NH * HD)), 'scales_k': small(ks[2], (H // GS, NKV * HD)), 'scales_v': small(ks[3], (H // GS, NKV * HD)), 'scales_o': small(ks[4], (NH * HD // GS, H)), 'qw_q': jax.random.randint(ks[5], (H, NH * HD), 0, 2 ** WBITS, jnp.int32), 'qw_k': jax.random.randint(ks[6], (H, NKV * HD), 0, 2 ** WBITS, jnp.int32), 'qw_v': jax.random.randint(ks[7], (H, NKV * HD), 0, 2 ** WBITS, jnp.int32), 'qw_o': jax.random.randint(ks[8], (NH * HD, H), 0, 2 ** WBITS, jnp.int32)}
    _L0_attn_in = _L0_attn_setup()

    def _L0_ffn_setup():
        import jax, jax.numpy as jnp
        import numpy as np
        D_IN = 512
        D_OUT = 512
        RANK = 16
        NUM_EXPERTS = 8
        TOP_K = 2
        SCALING = 32.0 / RANK
        key = jax.random.key(seed)
        ks = jax.random.split(key, 6)
        x = jax.random.normal(ks[0], (4, 256, D_IN), dtype=jnp.float32)
        W_base = jax.random.normal(ks[1], (D_OUT, D_IN), dtype=jnp.float32) * (1.0 / np.sqrt(D_IN))
        b_base = jax.random.normal(ks[2], (D_OUT,), dtype=jnp.float32) * 0.01
        W_router = jax.random.normal(ks[3], (NUM_EXPERTS, D_IN), dtype=jnp.float32) * 0.01
        A_stack = jax.random.uniform(ks[4], (NUM_EXPERTS, RANK, D_IN), dtype=jnp.float32, minval=-1.0, maxval=1.0) * (1.0 / np.sqrt(D_IN))
        B_stack = jax.random.normal(ks[5], (NUM_EXPERTS, D_OUT, RANK), dtype=jnp.float32) * 0.02
        return {'x': x, 'W_base': W_base, 'b_base': b_base, 'W_router': W_router, 'A_stack': A_stack, 'B_stack': B_stack}
    _L0_ffn_in = _L0_ffn_setup()
    _d = {'L0_attn_hidden_states': _L0_attn_in['hidden_states'], 'L0_attn_scales_q': _L0_attn_in['scales_q'], 'L0_attn_scales_k': _L0_attn_in['scales_k'], 'L0_attn_scales_v': _L0_attn_in['scales_v'], 'L0_attn_scales_o': _L0_attn_in['scales_o'], 'L0_attn_qw_q': _L0_attn_in['qw_q'], 'L0_attn_qw_k': _L0_attn_in['qw_k'], 'L0_attn_qw_v': _L0_attn_in['qw_v'], 'L0_attn_qw_o': _L0_attn_in['qw_o'], 'L0_ffn_W_base': _L0_ffn_in['W_base'], 'L0_ffn_b_base': _L0_ffn_in['b_base'], 'L0_ffn_W_router': _L0_ffn_in['W_router'], 'L0_ffn_A_stack': _L0_ffn_in['A_stack'], 'L0_ffn_B_stack': _L0_ffn_in['B_stack']}
    _x0 = _d['L0_attn_hidden_states']
    _d['L0_attn_hidden_states'] = jax.random.normal(jax.random.fold_in(jax.random.key(seed), 1), (2, 1024, 512), dtype=_x0.dtype)
    del _x0
    return _d

def reference(L0_attn_hidden_states, L0_attn_scales_q, L0_attn_scales_k, L0_attn_scales_v, L0_attn_scales_o, L0_attn_qw_q, L0_attn_qw_k, L0_attn_qw_v, L0_attn_qw_o, L0_ffn_W_base, L0_ffn_b_base, L0_ffn_W_router, L0_ffn_A_stack, L0_ffn_B_stack):

    def _L0_attn_ref(hidden_states, scales_q, scales_k, scales_v, scales_o, qw_q, qw_k, qw_v, qw_o):
        import jax, jax.numpy as jnp
        import numpy as np
        import math
        B, S, H = (1, 256, 512)
        NH, NKV, HD = (32, 8, 128)
        GS = 128
        WBITS = 4
        ZERO = float(2 ** (WBITS - 1))
        THETA = 10000.0

        def _dequant_matmul(x, qw, scales):
            w = (qw.astype(jnp.float32) - ZERO) * jnp.repeat(scales, GS, axis=0)
            return x @ w

        def _rope_tables(seq_len, dtype):
            inv_freq = 1.0 / THETA ** (jnp.arange(0, HD, 2, dtype=jnp.float32) / HD)
            freqs = jnp.arange(seq_len, dtype=jnp.float32)[:, None] * inv_freq
            emb = jnp.concatenate([freqs, freqs], axis=-1)
            return (jnp.cos(emb).astype(dtype), jnp.sin(emb).astype(dtype))

        def _rotate_half(x):
            x1, x2 = jnp.split(x, 2, axis=-1)
            return jnp.concatenate([-x2, x1], axis=-1)

        def _apply_rope(x, cos, sin):
            return x * cos[None, None] + _rotate_half(x) * sin[None, None]
        b, s, _ = hidden_states.shape
        q = _dequant_matmul(hidden_states, qw_q, scales_q).reshape(b, s, NH, HD).transpose(0, 2, 1, 3)
        k = _dequant_matmul(hidden_states, qw_k, scales_k).reshape(b, s, NKV, HD).transpose(0, 2, 1, 3)
        v = _dequant_matmul(hidden_states, qw_v, scales_v).reshape(b, s, NKV, HD).transpose(0, 2, 1, 3)
        cos, sin = _rope_tables(s, hidden_states.dtype)
        q = _apply_rope(q, cos, sin)
        k = _apply_rope(k, cos, sin)
        rep = NH // NKV
        k = jnp.repeat(k, rep, axis=1)
        v = jnp.repeat(v, rep, axis=1)
        scores = jnp.einsum('bhqd,bhkd->bhqk', q, k) / math.sqrt(HD)
        causal = jnp.tril(jnp.ones((s, s), dtype=bool))
        scores = jnp.where(causal[None, None], scores, jnp.finfo(scores.dtype).min)
        attn = jax.nn.softmax(scores.astype(jnp.float32), axis=-1).astype(q.dtype)
        ctx = jnp.einsum('bhqk,bhkd->bhqd', attn, v)
        ctx = ctx.transpose(0, 2, 1, 3).reshape(b, s, NH * HD)
        return _dequant_matmul(ctx, qw_o, scales_o)

    def _L0_ffn_ref(x, W_base, b_base, W_router, A_stack, B_stack):
        import jax, jax.numpy as jnp
        import numpy as np
        D_IN = 512
        D_OUT = 512
        RANK = 16
        NUM_EXPERTS = 8
        TOP_K = 2
        SCALING = 32.0 / RANK
        orig_shape = x.shape
        xf = x.reshape(-1, D_IN)
        logits = xf @ W_router.T
        probs = jax.nn.softmax(logits, axis=-1)
        topk_p, topk_i = jax.lax.top_k(probs, TOP_K)
        topk_p = topk_p / jnp.sum(topk_p, axis=-1, keepdims=True)
        combine = jnp.sum(jax.nn.one_hot(topk_i, NUM_EXPERTS, dtype=xf.dtype) * topk_p[..., None], axis=1)
        h = jnp.einsum('nd,erd->ner', xf, A_stack)
        h = h * combine[..., None]
        lora_out = jnp.einsum('ner,eor->no', h, B_stack) * SCALING
        base_out = xf @ W_base.T + b_base
        out = base_out + lora_out
        return out.reshape(orig_shape[:-1] + (D_OUT,))
    x = L0_attn_hidden_states
    xn = _layernorm(x, axis=-1)
    x = x + _L0_attn_ref(xn, L0_attn_scales_q, L0_attn_scales_k, L0_attn_scales_v, L0_attn_scales_o, L0_attn_qw_q, L0_attn_qw_k, L0_attn_qw_v, L0_attn_qw_o) + _L0_ffn_ref(xn, L0_ffn_W_base, L0_ffn_b_base, L0_ffn_W_router, L0_ffn_A_stack, L0_ffn_B_stack)
    return x

_drawn_inputs = setup_inputs


def setup_inputs(seed=0):
    import zlib

    import numpy as np

    out = dict(_drawn_inputs(seed))
    spreads = {}
    factors = {'L0_attn_scales_q': 3.421, 'L0_attn_scales_k': 3.419, 'L0_ffn_b_base': 8.0}
    for name, (base, spread) in spreads.items():
        noise = np.random.default_rng([zlib.crc32(name.encode()), seed]).standard_normal(out[name].shape)
        drawn = base * np.exp(spread * noise) if base else spread * noise
        out[name] = jnp.asarray(drawn.astype(out[name].dtype))
    for name, factor in factors.items():
        out[name] = (out[name] * factor).astype(out[name].dtype)
    return out
```

```python
import concourse.bass as bass
from concourse import mybir
from contextlib import ExitStack
import numpy as np

P = 128
BATCH, TOKENS, HID = 2, 1024, 512
NT = TOKENS // P
KT = HID // P
HALF = 512
NKV, REP = 8, 4
NEXP, RANK = 8, 16
ER = NEXP * RANK
AR = ER + NEXP
ZERO = 8.0
EPS = 1e-5
SCALING = 2.0
MASKED = -3.0e38

WEIGHTS = ["k", "q0", "v", "q1", "q2", "q3", "o0", "o1", "o2", "o3"]
INPUTS = WEIGHTS[:6]
OUTPUTS = WEIGHTS[6:]
PREPARED_WITH_HEAD = [["o0", "o1"], ["o2", "o3", "k"], ["q0", "v", "q1"], ["q2", "q3"]]


def unit_steps():
    def attend(h, c):
        n = 4 * (c + 1)
        steps = [("turn", h, c, 0), ("turn", h, c, 1)]
        for j in range(n):
            if j == n - 1:
                steps.append(("spread", h, c))
            steps.append(("values", h, c, j))
            if j + 2 < n:
                steps.append(("turn", h, c, j + 2))
        return steps + [("norm", h, c)]

    def merge(main, others):
        out, at = [], 0
        for pos, step in others:
            out += main[at:pos]
            at = pos
            out.append(step)
        return out + main[at:]

    steps = [("project", "k", 0), ("project", "k", 1), ("rotate", "k", 0), ("project", "q0", 0), ("rotate", "k", 1),
             ("project", "q0", 1), ("rotate", "q0", 0), ("rotate", "q0", 1), ("project", "v", 0), ("project", "v", 1)]
    steps += [("scores", 0, 0), ("scores", 0, 1), ("turn_v", 0), ("scores", 0, 2), ("turn_v", 1), ("scores", 0, 3)]
    for h in range(REP):
        extra = [(1, ("scores", h, 5)), (3, ("scores", h, 6)), (6, ("scores", h, 7))]
        if h + 1 < REP:
            w = f"q{h + 1}"
            extra = [(1, ("scores", h, 5)), (2, ("project", w, 0)), (4, ("project", w, 1)), (5, ("scores", h, 6)),
                     (5, ("rotate", w, 0)), (7, ("scores", h, 7)), (9, ("rotate", w, 1))]
        if h:
            extra.insert(0, (1, ("context", h - 1, 1)))
        steps += [("scores", h, 4)] + merge(attend(h, 0), extra)
        if h + 1 < REP:
            extra = [(0, ("scores", h + 1, 0)), (1, ("scores", h + 1, 1)), (2, ("context", h, 0)),
                     (4, ("scores", h + 1, 2)), (8, ("scores", h + 1, 3))]
        else:
            extra = [(1, ("context", h, 0)), (3, ("output", 0)), (5, ("output", 1)), (7, ("output", 2)),
                     (10, ("output", 3))]
        body = merge(attend(h, 1), extra)
        for n, w in enumerate(PREPARED_WITH_HEAD[h]):
            body.insert(5 * n + 4, ("scale", w))
            body.insert(5 * n + 7, ("split", w))
        steps += body
    steps += [("context", REP - 1, 1)]
    steps += [("output", t) for t in range(4, NT)]
    return steps


def ring_uses(steps):
    uses, item, made = {}, 0, {"scored": 0, "read": 2}
    order = [("read", 1), ("read", 2)]
    for s in steps:
        if s[0] == "scores" or s[0] == "project" and s[2] == 0 or s[0] == "output" and s[1] % 2 == 0:
            kind = "scored" if s[0] == "scores" else "read"
            made[kind] += 1
            uses[s] = (item % 2, order[item])
            order.append((kind, made[kind]))
            item += 1
        elif s[0] in ("project", "output"):
            uses[s] = ((item - 1) % 2, None)
    assert item % 2 == 0
    return uses


class Count:

    def __init__(self):
        self.seen = {}

    def next(self, sem, n=1):
        return self.upto(sem, self.seen.get(sem.num, (sem, 0))[1] + n)

    def upto(self, sem, value):
        self.seen[sem.num] = (sem, max(value, self.seen.get(sem.num, (sem, 0))[1]))
        return value

    def give_back(self, engine):
        for sem, value in self.seen.values():
            engine.sem_inc(sem, -value)
        self.seen = {}


def build_program(nc, x, scales_q, scales_k, scales_v, scales_o, qw_q, qw_k, qw_v, qw_o,
                  w_base_t, b_base, ar_t, b_t, rope_cos, rope_sin, eye, mask, expert_ids, out):
    f32, f32r, bf16 = mybir.dt.float32, mybir.dt.float32r, mybir.dt.bfloat16
    i32, u32 = mybir.dt.int32, mybir.dt.uint32
    ALU, ACT, AX = mybir.AluOpType, mybir.ActivationFunctionType, mybir.AxisListType

    STEPS = unit_steps()
    RING = ring_uses(STEPS)

    columns = {"k": (qw_k, scales_k, 1, 0), "v": (qw_v, scales_v, 1, 0)}
    columns |= {f"q{h}": (qw_q, scales_q, REP, h) for h in range(REP)}

    ctx = ExitStack()
    with ctx:
        def sb(name, shape, dt=f32):
            return ctx.enter_context(nc.sbuf_tensor(name, shape, dt))

        def sem(name):
            return ctx.enter_context(nc.semaphore(name))

        xnT_high = sb("xnT_high", [P, KT, TOKENS], f32r)
        xnT_low = sb("xnT_low", [P, KT, TOKENS], f32r)
        Y = sb("Y", [P, NT, HID])
        W_high = sb("W_high", [P, len(WEIGHTS), HID], f32r)
        W_low = sb("W_low", [P, len(WEIGHTS), HID], f32r)
        K_high = sb("K_high", [P, TOKENS], f32r)
        K_low = sb("K_low", [P, TOKENS], f32r)
        Q_high = sb("Q_high", [P, TOKENS], f32r)
        Q_low = sb("Q_low", [P, TOKENS], f32r)
        V_high = sb("V_high", [P, NT, P], f32r)
        V_low = sb("V_low", [P, NT, P], f32r)
        prob_at = [P * i * (i + 1) // 2 for i in range(NT + 1)]
        probs = sb("probs", [P, prob_at[NT]])
        PT_high = sb("PT_high", [P, 2, HALF], f32r)
        PT_low = sb("PT_low", [P, 2, HALF], f32r)
        ctx_high = sb("ctx_high", [P, REP, TOKENS], f32r)
        ctx_low = sb("ctx_low", [P, REP, TOKENS], f32r)
        cos_sb = sb("cos_sb", [P, TOKENS])
        sin_sb = sb("sin_sb", [P, TOKENS])
        rope_a = sb("rope_a", [P, 2, HALF])
        rope_b = sb("rope_b", [P, 2, HALF])
        raw = sb("raw", [P, 2, HID], i32)
        scl = sb("scl", [P, 2, HID])
        R_sb = sb("R_sb", [P, HALF])
        ctx_f = sb("ctx_f", [P, HALF])
        ident = sb("ident", [P, P])
        ident_b = sb("ident_b", [P, P], bf16)
        mask_b = sb("mask_b", [P, P], bf16)
        ones_r = sb("ones_r", [1, P], f32r)
        negmax = sb("negmax", [P, NT])
        sums = sb("sums", [P, NT])
        rinv = sb("rinv", [P, NT])
        stats = sb("stats", [P, NT, 6])
        mv = sb("mv", [P, NT, 2])
        var = sb("var", [P, NT])
        rstd = sb("rstd", [P, NT])
        newton = sb("newton", [P, NT])
        ids = sb("ids", [P, NEXP])
        route = sb("route", [P, 4, NT, NEXP])
        best = sb("best", [P, NT, 8])
        best_at = sb("best_at", [P, NT, 8], u32)
        best_id = sb("best_id", [P, NT, 8])
        column = sb("column", [P, 2, NT])

        lin_high = ctx_high[:, :, :].rearrange("p a b -> p (a b)")
        lin_low = ctx_low[:, :, :].rearrange("p a b -> p (a b)")
        LIN = {"base": (0, KT * HID), "ar": (KT * HID, KT * AR), "b": (KT * HID + KT * AR, HID)}
        lin_bias = KT * HID + KT * AR + HID
        lin_raw = probs[:, 2 * HID:2 * HID + lin_bias]
        bias_raw = R_sb[0:1, :]
        xn = probs[:, 0:2 * HID].rearrange("p (n h) -> p n h", n=2)
        hidden = rope_a[:, :, :].rearrange("p a b -> p (a b)")
        hid_lo = sb("hid_logits", [P, NT, NEXP])
        hT_high = PT_high[:, :, :].rearrange("p a b -> p (a b)").rearrange("p (t n) -> p t n", t=NT)
        hT_low = PT_low[:, :, :].rearrange("p a b -> p (a b)").rearrange("p (t n) -> p t n", t=NT)
        VT = probs[:, prob_at[4]:prob_at[4] + TOKENS]

        ring = [ctx.enter_context(nc.psum_tensor(f"ring{n}", [P, 2, HALF], f32)) for n in range(2)]
        turned_ps = [ctx.enter_context(nc.psum_tensor(f"turned{n}", [P, HALF], f32)) for n in range(2)]
        O_ps = ctx.enter_context(nc.psum_tensor("O_ps", [P, HALF], f32))
        gen_ps = ctx.enter_context(nc.psum_tensor("gen_ps", [P, HALF], f32))

        ring_full = sem("ring_full")
        ring_scored = sem("ring_scored")
        ring_read = sem("ring_read")
        negmax_ready = sem("negmax_ready")
        turned = sem("turned")
        pt_high = sem("pt_high")
        pt_low = sem("pt_low")
        o_full = sem("o_full")
        o_free = sem("o_free")
        rinv_ready = sem("rinv_ready")
        gen_full = sem("gen_full")
        gen_high = sem("gen_high")
        v_ready = sem("v_ready")
        rope_terms = sem("rope_terms")
        rope_sum = sem("rope_sum")
        rope_high = sem("rope_high")
        rope_done = sem("rope_done")
        terms_free = sem("terms_free")
        ctx_made = sem("ctx_made")
        ctx_high_done = sem("ctx_high_done")
        ctx_done = sem("ctx_done")
        ctx_f_free = sem("ctx_f_free")
        w_loaded = [sem(f"w_loaded{n}") for n in range(2)]
        w_free = sem("w_free")
        w_scaled = sem("w_scaled")
        w_high = sem("w_high")
        w_done = sem("w_done")
        const_loaded = sem("const_loaded")
        consts_ready = sem("consts_ready")
        x_loaded = sem("x_loaded")
        lin_loaded = sem("lin_loaded")
        lin_high_done = sem("lin_high_done")
        lin_done = sem("lin_done")
        var_ready = sem("var_ready")
        sqrt_done = sem("sqrt_done")
        xn_ready = sem("xn_ready")
        logits_ready = sem("logits_ready")
        route_exp = sem("route_exp")
        y_done = sem("y_done")
        stored = sem("stored")
        dve_own = sem("dve_own")
        pool_own = sem("pool_own")

        def weight_source(w, g):
            if w[0] == "o":
                h = g * REP + int(w[1])
                return (qw_o.rearrange("(h p) n -> h p n", p=P)[bass.ds(h, 1)].rearrange("a p n -> (a p) n"),
                        scales_o[bass.ds(h, 1), :].to_broadcast([P, HID]))
            q, s, rep, h = columns[w]
            at = bass.ds((g * rep + h) * P, P)
            return (q.rearrange("(k p) n -> p k n", p=P)[:, :, at],
                    s.rearrange("(a k) n -> a k n", a=1)[:, :, at].to_broadcast([P, KT, P]))

        block = ctx.enter_context(nc.Block())

        @block.sync
        def _(sp):
            count = Count()

            def load_weight(n, w, g):
                sp.wait_ge(w_free, count.next(w_free))
                src, scales = weight_source(w, g)
                dst, sdst = raw[:, n % 2, :], scl[:, n % 2, :]
                if w[0] != "o":
                    dst = dst.rearrange("p (k n) -> p k n", k=KT)
                    sdst = sdst.rearrange("p (k n) -> p k n", k=KT)
                sp.dma_start(dst, src).then_inc(w_loaded[n % 2], 16)
                sp.dma_start(sdst, scales).then_inc(w_loaded[n % 2], 16)

            for dst, src in ((ident, eye), (ctx_f[:, 0:P], mask), (ids, expert_ids), (cos_sb, rope_cos),
                             (sin_sb, rope_sin)):
                sp.dma_start(dst[:, :], src).then_inc(const_loaded, 16)
            for n, w in enumerate(INPUTS):
                load_weight(n, w, 0)
            count.give_back(sp)
            with sp.Fori(0, BATCH) as b:
                with sp.Fori(0, NKV) as g:
                    for n, w in enumerate(OUTPUTS + INPUTS):
                        load_weight(n, w, g if w in OUTPUTS else (g + 1) % NKV)
                    count.give_back(sp)
                sp.wait_ge(y_done, 1)
                sp.sem_inc(y_done, -1)
                sp.dma_start(out.rearrange("b (t p) h -> b p t h", p=P)[bass.ds(b, 1)]
                             .rearrange("a p t h -> (a p) t h"), Y[:, :, :]).then_inc(stored, 16)

        @block.gpsimd
        def _(pool):
            count = Count()

            def own(instruction):
                instruction.then_inc(pool_own, 1)
                pool.wait_ge(pool_own, count.next(pool_own))

            def scale_weight(n, w, alone=False):
                pool.wait_ge(w_loaded[n % 2], count.next(w_loaded[n % 2], 32))
                as_float = raw[:, n % 2, :].bitcast(f32)
                own(nc.gpsimd.tensor_scalar(as_float, raw[:, n % 2, :], -ZERO, 1.0, ALU.add, ALU.mult))
                scaled = nc.gpsimd.tensor_tensor(out=scl[:, n % 2, :], in0=as_float, in1=scl[:, n % 2, :],
                                                 op=ALU.mult)
                if alone:
                    own(scaled)
                else:
                    scaled.then_inc(w_scaled, 1)

            def split_weight(n, w, alone=False):
                slot = WEIGHTS.index(w)
                if alone:
                    own(nc.gpsimd.tensor_scalar(W_high[:, slot, :], scl[:, n % 2, :], 0.0, 1.0, ALU.add, ALU.mult))
                else:
                    pool.wait_ge(w_high, count.next(w_high))
                own(nc.gpsimd.tensor_tensor(out=W_low[:, slot, :], in0=scl[:, n % 2, :],
                                            in1=W_high[:, slot, :].bitcast(f32), op=ALU.subtract))
                pool.sem_inc(w_done, 1)
                pool.sem_inc(w_free, 1)

            def rope_add(c):
                pool.wait_ge(rope_terms, count.next(rope_terms))
                nc.gpsimd.tensor_tensor(out=rope_a[:, c, :], in0=rope_a[:, c, :], in1=rope_b[:, c, :],
                                        op=ALU.add).then_inc(rope_sum, 1)

            def rope_low(dst_high, dst_low, c):
                pool.wait_ge(rope_high, count.next(rope_high))
                at = slice(c * HALF, (c + 1) * HALF)
                own(nc.gpsimd.tensor_tensor(out=dst_low[:, at], in0=rope_a[:, c, :],
                                            in1=dst_high[:, at].bitcast(f32), op=ALU.subtract))
                pool.sem_inc(rope_done, 1)
                pool.sem_inc(terms_free, 1)

            def split_context(h, c):
                pool.wait_ge(ctx_high_done, count.next(ctx_high_done))
                at = slice(c * HALF, (c + 1) * HALF)
                own(nc.gpsimd.tensor_tensor(out=ctx_low[:, h, at], in0=ctx_f[:, :],
                                            in1=ctx_high[:, h, at].bitcast(f32), op=ALU.subtract))
                pool.sem_inc(ctx_done, 1)
                pool.sem_inc(ctx_f_free, 1)

            pool.sem_inc(w_free, 2)
            pool.sem_inc(terms_free, 2)
            pool.sem_inc(ctx_f_free, 1)
            for n, w in enumerate(INPUTS):
                scale_weight(n, w, alone=True)
                split_weight(n, w, alone=True)
            count.give_back(pool)
            with pool.Fori(0, BATCH):
                with pool.Fori(0, NKV):
                    order = OUTPUTS + INPUTS
                    for step in STEPS:
                        kind, *of = step
                        if kind == "project" and of[0] != "v":
                            rope_add(of[1])
                        elif kind == "rotate":
                            rope_low(*((K_high, K_low) if of[0] == "k" else (Q_high, Q_low)), of[1])
                        elif kind == "context":
                            split_context(of[0], of[1])
                        elif kind == "scale":
                            scale_weight(order.index(of[0]), of[0])
                        elif kind == "split":
                            split_weight(order.index(of[0]), of[0])
                    count.give_back(pool)

        @block.scalar
        def _(act):
            count = Count()

            def copy(dst, src):
                return nc.scalar.activation(dst, src, ACT.Copy)

            def weight_high(n, w):
                act.wait_ge(w_scaled, count.next(w_scaled))
                copy(W_high[:, WEIGHTS.index(w), :], scl[:, n % 2, :]).then_inc(w_high, 1)

            def batch_start(b):
                act.wait_ge(stored, count.next(stored, 16))
                for name, src in (("base", w_base_t), ("ar", ar_t), ("b", b_t)):
                    at, n = LIN[name]
                    dst = lin_raw[:, at:at + n]
                    if name != "b":
                        src, dst = src.rearrange("(k p) n -> p k n", p=P), dst.rearrange("p (k n) -> p k n", k=KT)
                    act.dma_start(dst, src).then_inc(lin_loaded, 16)
                act.dma_start(bias_raw, b_base).then_inc(lin_loaded, 16)
                act.dma_start(Y[:, :, :], x.rearrange("b (t p) h -> b p t h", p=P)[bass.ds(b, 1)]
                              .rearrange("a p t h -> (a p) t h")).then_inc(x_loaded, 16)
                act.wait_ge(lin_loaded, count.next(lin_loaded, 64))
                for at, size in LIN.values():
                    copy(lin_high[:, at:at + size], lin_raw[:, at:at + size]).then_inc(lin_high_done, 1)
                copy(lin_high[0:1, lin_bias:lin_bias + HID], bias_raw).then_inc(lin_high_done, 1)
                act.wait_ge(var_ready, count.next(var_ready))
                nc.scalar.activation(rstd[:, :], var[:, :], ACT.Sqrt).then_inc(sqrt_done, 1)
                for t in range(NT):
                    act.wait_ge(turned, count.next(turned))
                    copy(xnT_high[:, :, t * P:(t + 1) * P],
                         turned_ps[t % 2][:, :].rearrange("p (k n) -> p k n", k=KT)).then_inc(pt_high, 1)
                act.wait_ge(logits_ready, count.next(logits_ready))
                nc.scalar.activation(route[:, 1, :, :], route[:, 0, :, :], ACT.Exp).then_inc(route_exp, 1)
                for n in range(2):
                    act.wait_ge(turned, count.next(turned))
                    copy(hT_high[:, 4 * n:4 * n + 4, :],
                         turned_ps[n][:, :].rearrange("p (t n) -> p t n", t=4)).then_inc(pt_high, 1)

            act.sem_inc(stored, 16)
            with act.Fori(0, BATCH) as b:
                batch_start(b)
                count.give_back(act)
                with act.Fori(0, NKV):
                    order = OUTPUTS + INPUTS
                    for step in STEPS:
                        kind, *of = step
                        if kind == "rotate":
                            w, c = of
                            act.wait_ge(rope_sum, count.next(rope_sum))
                            dst = K_high if w == "k" else Q_high
                            copy(dst[:, c * HALF:(c + 1) * HALF], rope_a[:, c, :]).then_inc(rope_high, 1)
                        elif kind == "turn_v":
                            act.wait_ge(gen_full, count.next(gen_full))
                            copy(V_high[:, 4 * of[0]:4 * of[0] + 4, :],
                                 gen_ps[:, :].rearrange("p (t n) -> p t n", t=4)).then_inc(gen_high, 1)
                        elif kind == "scores":
                            h, i = of
                            n = (i + 1) * P
                            act.wait_ge(negmax_ready, count.next(negmax_ready))
                            nc.scalar.activation(
                                probs[:, prob_at[i]:prob_at[i] + n],
                                ring[RING[step][0]][:, :, :].rearrange("p a b -> p (a b)")[:, 0:n], ACT.Exp,
                                bias=negmax[:, i:i + 1], accum_out=sums[:, i:i + 1]).then_inc(ring_scored, 1)
                        elif kind == "turn":
                            h, c, j = of
                            at = slice(max(0, j - 4 * c) * P, HALF)
                            act.wait_ge(turned, count.next(turned))
                            copy(PT_high[:, j % 2, at], turned_ps[j % 2][:, at]).then_inc(pt_high, 1)
                        elif kind == "spread":
                            act.wait_ge(gen_full, count.next(gen_full))
                            copy(R_sb[:, :], gen_ps[:, :]).then_inc(gen_high, 1)
                        elif kind == "context":
                            h, c = of
                            act.wait_ge(ctx_made, count.next(ctx_made))
                            copy(ctx_high[:, h, c * HALF:(c + 1) * HALF], ctx_f[:, :]).then_inc(ctx_high_done, 1)
                        elif kind == "split":
                            weight_high(order.index(of[0]), of[0])
                    count.give_back(act)
            act.wait_ge(stored, 16)

        @block.vector
        def _(dve):
            count = Count()

            def own(instruction):
                instruction.then_inc(dve_own, 1)
                dve.wait_ge(dve_own, count.next(dve_own))

            def linear_weights():
                for at, size in LIN.values():
                    dve.wait_ge(lin_high_done, count.next(lin_high_done))
                    nc.vector.tensor_tensor(out=lin_low[:, at:at + size], in0=lin_raw[:, at:at + size],
                                            in1=lin_high[:, at:at + size].bitcast(f32), op=ALU.subtract)
                dve.wait_ge(lin_high_done, count.next(lin_high_done))
                at = slice(lin_bias, lin_bias + HID)
                nc.vector.tensor_tensor(out=lin_low[0:1, at], in0=bias_raw, in1=lin_high[0:1, at].bitcast(f32),
                                        op=ALU.subtract).then_inc(lin_done, 1)

            def layer_norm_stats():
                dve.wait_ge(x_loaded, count.next(x_loaded, 16))
                for t in range(NT):
                    last = nc.vector.bn_stats(stats[:, t, :], Y[:, t, :])
                own(last)
                for t in range(NT):
                    last = nc.vector.bn_aggr(mv[:, t, :], stats[:, t, :])
                own(last)
                nc.vector.tensor_scalar_add(var[:, :], mv[:, :, 1], EPS).then_inc(var_ready, 1)
                dve.wait_ge(sqrt_done, count.next(sqrt_done))
                own(nc.vector.reciprocal(rstd[:, :], rstd[:, :]))
                own(nc.vector.tensor_tensor(out=newton[:, :], in0=rstd[:, :], in1=rstd[:, :], op=ALU.mult))
                own(nc.vector.tensor_tensor(out=newton[:, :], in0=newton[:, :], in1=var[:, :], op=ALU.mult))
                own(nc.vector.tensor_scalar(newton[:, :], newton[:, :], -0.5, 1.5, ALU.mult, ALU.add))
                own(nc.vector.tensor_tensor(out=rstd[:, :], in0=rstd[:, :], in1=newton[:, :], op=ALU.mult))

            def normalise(t):
                nc.vector.tensor_scalar(xn[:, t % 2, :], Y[:, t, :], mv[:, t, 0:1], rstd[:, t:t + 1],
                                        ALU.subtract, ALU.mult).then_inc(xn_ready, 1)

            def xn_low(t):
                dve.wait_ge(pt_high, count.next(pt_high))
                at = slice(t * P, (t + 1) * P)
                nc.vector.tensor_tensor(out=xnT_low[:, :, at],
                                        in0=turned_ps[t % 2][:, :].rearrange("p (k n) -> p k n", k=KT),
                                        in1=xnT_high[:, :, at].bitcast(f32), op=ALU.subtract).then_inc(pt_low, 1)

            def linear_read(t):
                dve.wait_ge(ring_full, count.next(ring_full))
                ps = ring[t % 2]
                nc.vector.tensor_tensor(out=Y[:, t, :], in0=ps[:, 0, :], in1=Y[:, t, :], op=ALU.add)
                nc.vector.tensor_copy(hidden[:, t * ER:(t + 1) * ER], ps[:, 1, 0:ER])
                last = nc.vector.tensor_copy(hid_lo[:, t, :], ps[:, 1, ER:AR])
                if t < NT - 1:
                    last.then_inc(ring_read, 1)
                else:
                    own(last)
                    dve.sem_inc(ring_read, 1)

            def routing():
                logits, probs_e = route[:, 0, :, :], route[:, 1, :, :]
                one_hot, combine = route[:, 2, :, :], route[:, 3, :, :]

                def by_tile(ap):
                    return ap.unsqueeze(2).to_broadcast([P, NT, NEXP])

                def over_tiles(ap):
                    return ap.unsqueeze(1).to_broadcast([P, NT, NEXP])

                own(nc.vector.tensor_reduce(column[:, 0, :], hid_lo[:, :, :], op=ALU.max, axis=AX.X))
                nc.vector.tensor_tensor(out=logits, in0=hid_lo[:, :, :], in1=by_tile(column[:, 0, :]),
                                        op=ALU.subtract).then_inc(logits_ready, 1)
                dve.wait_ge(route_exp, count.next(route_exp))
                own(nc.vector.tensor_reduce(column[:, 0, :], probs_e, op=ALU.add, axis=AX.X))
                own(nc.vector.reciprocal(column[:, 0, :], column[:, 0, :]))
                own(nc.vector.tensor_tensor(out=probs_e, in0=probs_e, in1=by_tile(column[:, 0, :]), op=ALU.mult))
                for t in range(NT):
                    last = nc.vector.max(best[:, t, :], route[:, 1, t, :])
                own(last)
                for t in range(NT):
                    last = nc.vector.max_index(best_at[:, t, :], best[:, t, :], route[:, 1, t, :])
                own(last)
                own(nc.vector.tensor_copy(best_id[:, :, :], best_at[:, :, :]))
                own(nc.vector.tensor_tensor(out=column[:, 0, :], in0=best[:, :, 0], in1=best[:, :, 1], op=ALU.add))
                own(nc.vector.reciprocal(column[:, 0, :], column[:, 0, :]))
                for n in range(2):
                    own(nc.vector.tensor_tensor(out=column[:, 1, :], in0=best[:, :, n], in1=column[:, 0, :],
                                                op=ALU.mult))
                    own(nc.vector.tensor_scalar(column[:, 1, :], column[:, 1, :], SCALING, None, ALU.mult))
                    own(nc.vector.tensor_tensor(out=one_hot, in0=over_tiles(ids[:, :]),
                                                in1=by_tile(best_id[:, :, n]), op=ALU.is_equal))
                    dst = combine if n == 0 else one_hot
                    own(nc.vector.tensor_tensor(out=dst, in0=one_hot, in1=by_tile(column[:, 1, :]), op=ALU.mult))
                own(nc.vector.tensor_tensor(out=combine, in0=combine, in1=one_hot, op=ALU.add))
                h = hidden.rearrange("p (e r) -> p e r", r=RANK)
                nc.vector.tensor_tensor(
                    out=h, in0=h, in1=combine.rearrange("p t e -> p (t e)").unsqueeze(2)
                    .to_broadcast([P, NT * NEXP, RANK]), op=ALU.mult).then_inc(xn_ready, 1)

            def hidden_low(n):
                dve.wait_ge(pt_high, count.next(pt_high))
                nc.vector.tensor_tensor(out=hT_low[:, 4 * n:4 * n + 4, :],
                                        in0=turned_ps[n][:, :].rearrange("p (t n) -> p t n", t=4),
                                        in1=hT_high[:, 4 * n:4 * n + 4, :].bitcast(f32),
                                        op=ALU.subtract).then_inc(pt_low, 1)

            def lowrank_read(n):
                dve.wait_ge(ring_full, count.next(ring_full))
                nc.vector.tensor_tensor(out=Y[:, 2 * n:2 * n + 2, :], in0=ring[n % 2][:, :, :],
                                        in1=Y[:, 2 * n:2 * n + 2, :], op=ALU.add).then_inc(ring_read, 1)

            def rope_terms_of(step):
                c = step[2]
                at = slice(c * HALF, (c + 1) * HALF)
                ps = ring[RING[step][0]][:, c, :]
                dve.wait_ge(ring_full, count.next(ring_full))
                dve.wait_ge(terms_free, count.next(terms_free))
                nc.vector.tensor_tensor(out=rope_a[:, c, :], in0=ps, in1=cos_sb[:, at], op=ALU.mult)
                nc.vector.tensor_tensor(out=rope_b[0:64, c, :], in0=ps[64:128, :], in1=sin_sb[64:128, at],
                                        op=ALU.mult)
                last = nc.vector.tensor_tensor(out=rope_b[64:128, c, :], in0=ps[0:64, :], in1=sin_sb[0:64, at],
                                               op=ALU.mult)
                if c == 0:
                    last.then_inc(rope_terms, 1)
                else:
                    own(last)
                    dve.sem_inc(ring_read, 1)
                    dve.sem_inc(rope_terms, 1)

            dve.wait_ge(const_loaded, count.next(const_loaded, 80))
            nc.vector.tensor_copy(mask_b[:, :], ctx_f[:, 0:P])
            nc.vector.memset(ones_r[:, :].bitcast(f32), 1.0)
            nc.vector.tensor_copy(ident_b[:, :], ident[:, :]).then_inc(consts_ready, 1)
            dve.sem_inc(ring_read, 2)
            dve.sem_inc(o_free, 1)
            count.give_back(dve)
            with dve.Fori(0, BATCH):
                linear_weights()
                layer_norm_stats()
                normalise(0)
                normalise(1)
                for t in range(NT):
                    xn_low(t)
                    if t + 2 < NT:
                        normalise(t + 2)
                    if t >= 1:
                        linear_read(t - 1)
                linear_read(NT - 1)
                routing()
                for n in range(2):
                    hidden_low(n)
                for n in range(NT // 2):
                    lowrank_read(n)
                count.give_back(dve)
                with dve.Fori(0, NKV):
                    for step in STEPS:
                        kind, *of = step
                        if kind == "project":
                            w, c = of
                            if w != "v":
                                rope_terms_of(step)
                            else:
                                dve.wait_ge(ring_full, count.next(ring_full))
                                last = nc.vector.tensor_copy(VT[:, c * HALF:(c + 1) * HALF],
                                                             ring[RING[step][0]][:, c, :])
                                if c == 1:
                                    last.then_inc(ring_read, 1)
                        elif kind == "turn_v":
                            dve.wait_ge(gen_high, count.next(gen_high))
                            at = slice(4 * of[0], 4 * of[0] + 4)
                            nc.vector.tensor_tensor(out=V_low[:, at, :],
                                                    in0=gen_ps[:, :].rearrange("p (t n) -> p t n", t=4),
                                                    in1=V_high[:, at, :].bitcast(f32),
                                                    op=ALU.subtract).then_inc(v_ready, 1)
                        elif kind == "scores":
                            h, i = of
                            dve.wait_ge(ring_full, count.next(ring_full))
                            nc.vector.tensor_reduce(
                                negmax[:, i:i + 1],
                                ring[RING[step][0]][:, :, :].rearrange("p a b -> p (a b)")[:, 0:(i + 1) * P],
                                op=ALU.max, axis=AX.X, negate=True).then_inc(negmax_ready, 1)
                        elif kind == "turn":
                            h, c, j = of
                            at = slice(max(0, j - 4 * c) * P, HALF)
                            dve.wait_ge(pt_high, count.next(pt_high))
                            nc.vector.tensor_tensor(out=PT_low[:, j % 2, at], in0=turned_ps[j % 2][:, at],
                                                    in1=PT_high[:, j % 2, at].bitcast(f32),
                                                    op=ALU.subtract).then_inc(pt_low, 1)
                            if j == 0:
                                nc.vector.reciprocal(rinv[:, 4 * c:4 * c + 4],
                                                     sums[:, 4 * c:4 * c + 4]).then_inc(rinv_ready, 1)
                        elif kind == "norm":
                            dve.wait_ge(o_full, count.next(o_full))
                            dve.wait_ge(gen_high, count.next(gen_high))
                            dve.wait_ge(ctx_f_free, count.next(ctx_f_free))
                            own(nc.vector.tensor_tensor(out=ctx_f[:, :], in0=O_ps[:, :], in1=R_sb[:, :],
                                                        op=ALU.mult))
                            dve.sem_inc(o_free, 1)
                            dve.sem_inc(ctx_made, 1)
                        elif kind == "output":
                            t = of[0]
                            dve.wait_ge(ring_full, count.next(ring_full))
                            last = nc.vector.tensor_tensor(out=Y[:, t, :], in0=ring[RING[step][0]][:, t % 2, :],
                                                           in1=Y[:, t, :], op=ALU.add)
                            if t % 2:
                                last.then_inc(ring_read, 1)
                    count.give_back(dve)
                dve.drain().then_inc(y_done, 1)

        @block.tensor
        def _(pe):
            count = Count()

            def product(dst, pairs, start=True, stop=True):
                terms = [t for (lh, ll), (rh, rl) in pairs for t in ((lh, rh), (lh, rl), (ll, rh))]
                for n, (lhs, rhs) in enumerate(terms):
                    mm = nc.tensor.matmul(dst, lhs, rhs, start=start and n == 0, stop=stop and n == len(terms) - 1)
                return mm

            def both(high, low, *at):
                return high[at], low[at]

            def lin(name, lo=0, hi=None):
                at, size = LIN[name]
                hi = size if hi is None else hi
                return lin_high[:, at + lo:at + hi], lin_low[:, at + lo:at + hi]

            def turn_xn(t):
                pe.wait_ge(xn_ready, count.next(xn_ready))
                if t >= 2:
                    pe.wait_ge(pt_low, count.upto(pt_low, t - 1))
                for k in range(KT):
                    mm = nc.tensor.transpose(turned_ps[t % 2][:, k * P:(k + 1) * P], xn[:, t % 2, k * P:(k + 1) * P],
                                             ident[:, :])
                mm.then_inc(turned, 1)

            def linear(t):
                pe.wait_ge(pt_low, count.upto(pt_low, t + 1))
                pe.wait_ge(lin_done, count.upto(lin_done, 1))
                pe.wait_ge(ring_read, count.next(ring_read))
                ps, tile = ring[t % 2], slice(t * P, (t + 1) * P)
                xk = [both(xnT_high, xnT_low, slice(None), k, tile) for k in range(KT)]
                product(ps[:, 0, :], [(xk[k], lin("base", k * HID, (k + 1) * HID)) for k in range(KT)], stop=False)
                at = slice(lin_bias, lin_bias + HID)
                nc.tensor.matmul(ps[:, 0, :], ones_r[:, :], lin_high[0:1, at], start=False, stop=False)
                nc.tensor.matmul(ps[:, 0, :], ones_r[:, :], lin_low[0:1, at], start=False, stop=True)
                product(ps[:, 1, 0:AR], [(xk[k], lin("ar", k * AR, (k + 1) * AR)) for k in range(KT)])\
                    .then_inc(ring_full, 1)

            def turn_hidden(n):
                if n == 0:
                    pe.wait_ge(xn_ready, count.next(xn_ready))
                for t in range(4):
                    mm = nc.tensor.transpose(turned_ps[n][:, t * P:(t + 1) * P],
                                             hidden[:, (4 * n + t) * ER:(4 * n + t + 1) * ER], ident[:, :])
                mm.then_inc(turned, 1)

            def lowrank(n):
                pe.wait_ge(pt_low, count.upto(pt_low, NT + 1 + n // 2))
                pe.wait_ge(ring_read, count.next(ring_read))
                for t in (2 * n, 2 * n + 1):
                    mm = product(ring[n % 2][:, t % 2, :], [(both(hT_high, hT_low, slice(None), t), lin("b"))])
                mm.then_inc(ring_full, 1)

            def take_ring(step):
                freed = RING[step][1]
                if freed is not None and freed[0] == "scored":
                    pe.wait_ge(ring_scored, count.upto(ring_scored, freed[1]))
                elif freed is not None:
                    pe.wait_ge(ring_read, count.upto(ring_read, freed[1]))

            scored = {step[1:]: n + 1 for n, step in enumerate(s for s in STEPS if s[0] == "scores")}

            def project(step):
                _, w, c = step
                if c == 0:
                    pe.wait_ge(w_done, count.next(w_done))
                take_ring(step)
                slot = WEIGHTS.index(w)
                product(ring[RING[step][0]][:, c, :],
                        [(both(W_high, W_low, slice(None), slot, slice(k * P, (k + 1) * P)),
                          both(xnT_high, xnT_low, slice(None), k, slice(c * HALF, (c + 1) * HALF)))
                         for k in range(KT)]).then_inc(ring_full, 1)

            def turn_v(n):
                pe.wait_ge(ring_read, count.upto(ring_read, VT_READ))
                if n:
                    pe.wait_ge(v_ready, count.upto(v_ready, n))
                for t in range(4):
                    at = slice((4 * n + t) * P, (4 * n + t + 1) * P)
                    mm = nc.tensor.transpose(gen_ps[:, t * P:(t + 1) * P], VT[:, at], ident[:, :])
                mm.then_inc(gen_full, 1)

            def scores(step):
                _, h, i = step
                pe.wait_ge(rope_done, count.upto(rope_done, 2 + 2 * h + (1 if i < 4 else 2)))
                take_ring(step)
                ps = ring[RING[step][0]]
                n, tile = (i + 1) * P, slice(i * P, (i + 1) * P)
                banks = [(0, min(n, HALF))] + ([(HALF, n)] if n > HALF else [])
                for lhs, keys, first, last in ((Q_high, K_high, True, False), (Q_high, K_low, False, False),
                                               (Q_low, K_high, False, True)):
                    for b, (lo, hi) in enumerate(banks):
                        mm = nc.tensor.matmul(ps[:, b, 0:hi - lo], lhs[:, tile], keys[:, lo:hi],
                                              start=first, stop=last)
                        if first and hi == n:
                            nc.tensor.matmul(ps[:, b, hi - lo - P:hi - lo], ident_b[:, :], mask_b[:, :],
                                             start=False, stop=False)
                mm.then_inc(ring_full, 1)

            turn_number = {step[1:]: n + 1 for n, step in enumerate(s for s in STEPS if s[0] == "turn")}

            def turn(h, c, j):
                pe.wait_ge(ring_scored, count.upto(ring_scored, scored[(h, 4 * c + 3)]))
                if turn_number[(h, c, j)] > 2:
                    pe.wait_ge(pt_low, count.upto(pt_low, turn_number[(h, c, j)] - 2))
                for q in range(max(0, j - 4 * c), 4):
                    at = prob_at[4 * c + q] + j * P
                    mm = nc.tensor.transpose(turned_ps[j % 2][:, q * P:(q + 1) * P], probs[:, at:at + P],
                                             ident[:, :])
                mm.then_inc(turned, 1)

            def values(h, c, j):
                if j == 0:
                    pe.wait_ge(v_ready, count.upto(v_ready, 2))
                    pe.wait_ge(o_free, count.next(o_free))
                pe.wait_ge(pt_low, count.upto(pt_low, turn_number[(h, c, j)]))
                last_tile = j == 4 * c + 3
                at = slice(max(0, j - 4 * c) * P, HALF)
                pair = (both(V_high, V_low, slice(None), j), both(PT_high, PT_low, slice(None), j % 2, at))
                mm = product(O_ps[:, at], [pair], start=j == 0, stop=last_tile)
                if last_tile:
                    mm.then_inc(o_full, 1)

            def spread_sums(h, c):
                pe.wait_ge(rinv_ready, count.next(rinv_ready))
                for q in range(4):
                    n = 4 * c + q
                    mm = nc.tensor.transpose(gen_ps[:, q * P:(q + 1) * P],
                                             rinv[:, n:n + 1].to_broadcast([P, P]), ident[:, :])
                mm.then_inc(gen_full, 1)

            chunk_number = {step[1:3]: n + 1 for n, step in enumerate(s for s in STEPS if s[0] == "context")}

            def output(step):
                t = step[1]
                take_ring(step)
                if t == 0:
                    pe.wait_ge(w_done, count.next(w_done, REP))
                pe.wait_ge(ctx_done, count.upto(ctx_done, chunk_number[(REP - 1, t // 4)]))
                tile = slice(t * P, (t + 1) * P)
                product(ring[RING[step][0]][:, t % 2, :],
                        [(both(ctx_high, ctx_low, slice(None), h, tile),
                          both(W_high, W_low, slice(None), WEIGHTS.index(f"o{h}"))) for h in range(REP)])\
                    .then_inc(ring_full, 1)

            VT_READ = 2 + 3
            pe.wait_ge(consts_ready, 1)
            with pe.Fori(0, BATCH):
                turn_xn(0)
                for t in range(NT):
                    if t + 1 < NT:
                        turn_xn(t + 1)
                    linear(t)
                turn_hidden(0)
                turn_hidden(1)
                for n in range(NT // 2):
                    lowrank(n)
                count.give_back(pe)
                with pe.Fori(0, NKV):
                    for step in STEPS:
                        kind, *of = step
                        if kind == "project":
                            project(step)
                        elif kind == "turn_v":
                            turn_v(*of)
                        elif kind == "scores":
                            scores(step)
                        elif kind == "turn":
                            turn(*of)
                        elif kind == "values":
                            values(*of)
                        elif kind == "spread":
                            spread_sums(*of)
                        elif kind == "output":
                            output(step)
                    count.give_back(pe)



def rope_tables():
    inv = (1.0 / np.float32(10000.0) ** (np.arange(0, P, 2, dtype=np.float32) / np.float32(P))).astype(np.float32)
    freqs = np.arange(TOKENS, dtype=np.float32)[None, :] * inv[:, None]
    scale = float(P) ** -0.25
    cos, sin = np.cos(freqs.astype(np.float64)) * scale, np.sin(freqs.astype(np.float64)) * scale
    return np.concatenate([cos, cos]).astype(np.float32), np.concatenate([sin, -sin]).astype(np.float32)


def kernel(**inputs):
    import concourse.bacc as bacc
    from concourse.bass_utils import run_bass_kernel_spmd

    a = {n.split("_", 2)[2]: np.asarray(v) for n, v in inputs.items()}
    cos, sin = rope_tables()
    arrays = {
        "x": a["hidden_states"],
        "scales_q": a["scales_q"], "scales_k": a["scales_k"], "scales_v": a["scales_v"], "scales_o": a["scales_o"],
        "qw_q": a["qw_q"], "qw_k": a["qw_k"], "qw_v": a["qw_v"], "qw_o": a["qw_o"],
        "w_base_t": a["W_base"].T,
        "b_base": a["b_base"].reshape(1, HID),
        "ar_t": np.concatenate([a["A_stack"].reshape(ER, HID), a["W_router"]]).T,
        "b_t": a["B_stack"].transpose(0, 2, 1).reshape(ER, HID),
        "rope_cos": cos, "rope_sin": sin,
        "eye": np.eye(P, dtype=np.float32),
        "mask": np.triu(np.full((P, P), MASKED, np.float32), 1),
        "expert_ids": np.tile(np.arange(NEXP, dtype=np.float32), (P, 1)),
    }
    arrays = {f"in_{n}": np.ascontiguousarray(v) for n, v in arrays.items()}
    nc = bacc.Bacc("TRN2", target_bir_lowering=False, num_devices=1)
    args = [nc.dram_tensor(n, v.shape, mybir.dt.from_np(v.dtype), kind="ExternalInput").ap() for n, v in arrays.items()]
    out = nc.dram_tensor("out", (BATCH, TOKENS, HID), mybir.dt.float32, kind="ExternalOutput").ap()
    build_program(nc, *args, out)
    r = run_bass_kernel_spmd(nc, [arrays], core_ids=[0])
    return r.results[0]["out"]
```
